# Optimizing a Trainium2 kernel written in Bass

```python
import numpy as np
import jax
import jax.numpy as jnp

def _softmax(x, axis=-1):
    return jax.nn.softmax(x, axis=axis)

def _gelu(x):
    return jax.nn.gelu(x, approximate=True)

def _silu(x):
    return jax.nn.silu(x)

def _sigmoid(x):
    return jax.nn.sigmoid(x)

def _layernorm(x, axis=-1, eps=1e-05):
    m = jnp.mean(x, axis=axis, keepdims=True)
    v = jnp.var(x, axis=axis, keepdims=True)
    return (x - m) / jnp.sqrt(v + eps)

def _scatter_add(tgt, idx, src, axis=0):
    return tgt.at[idx].add(src)

def _segment_sum(src, seg, n):
    return jax.ops.segment_sum(src, seg, n)
kernel_name = 'mk_gnn_preln_d2_gnn_r16_6fbc54'

def setup_inputs(seed: int=0):
    np.random.seed(seed)
    _w = jnp.asarray

    def _rec_inputs():
        import jax
        import jax.numpy as jnp
        _gk = jax.random.key(seed)
        x = -0.000202 + 1 * jax.random.normal(jax.random.fold_in(_gk, 1), (6250, 64), jnp.float32)
        src = jax.random.randint(jax.random.fold_in(_gk, 2), (200000,), 0, 6250, jnp.int32)
        dst = jax.random.randint(jax.random.fold_in(_gk, 3), (200000,), 0, 6250, jnp.int32)
        _o = jnp.argsort(dst, stable=True)
        src = src[_o]
        dst = dst[_o]
        edge_attr_16 = 0.000312547 + 1.00004 * jax.random.normal(jax.random.fold_in(_gk, 11), (200000, 16), jnp.float32)
        return (x, src, dst, edge_attr_16)
    x, src, dst, edge_attr_16 = _rec_inputs()

    def _L0_gnn_setup():
        import jax, jax.numpy as jnp
        import numpy as np
        N = 6250
        E = 62500
        C = 64
        H = 4
        O = C // H
        NEG_SLOPE = 0.2

        def _gatv2_layer(x, src, dst, Wl, Wr, a, b):
            xl = (x @ Wl).reshape(N, H, O)
            xr = (x @ Wr).reshape(N, H, O)
            s = jax.nn.leaky_relu(xl[src] + xr[dst], NEG_SLOPE)
            e = jnp.einsum('eho,ho->eh', s, a)
            m = jax.ops.segment_max(e, dst, num_segments=N)
            ex = jnp.exp(e - m[dst])
            denom = jax.ops.segment_sum(ex, dst, num_segments=N)
            alpha = ex / (denom[dst] + 1e-16)
            out = jax.ops.segment_sum(xl[src] * alpha[:, :, None], dst, num_segments=N)
            return out.reshape(N, H * O) + b
        key = jax.random.key(seed)
        ks = jax.random.split(key, 14)
        x = jax.random.normal(ks[0], (N, C), dtype=jnp.float32)
        edge_index = jax.random.randint(ks[1], (2, E), 0, N, dtype=jnp.int64)
        s = 1.0 / np.sqrt(C)
        params = {}
        for l in range(3):
            params[f'Wl{l + 1}'] = jax.random.normal(ks[2 + 4 * l], (C, H * O), dtype=jnp.float32) * s
            params[f'Wr{l + 1}'] = jax.random.normal(ks[3 + 4 * l], (C, H * O), dtype=jnp.float32) * s
            params[f'a{l + 1}'] = jax.random.normal(ks[4 + 4 * l], (H, O), dtype=jnp.float32) * s
            params[f'b{l + 1}'] = jnp.zeros((H * O,), dtype=jnp.float32)
        return {'x': x, 'edge_index': edge_index, **params}
    _L0_gnn_all = _L0_gnn_setup()
    _L0_gnn_in = {k: v for k, v in _L0_gnn_all.items() if k in ('Wl1', 'Wr1', 'a1', 'b1', 'Wl2', 'Wr2', 'a2', 'b2', 'Wl3', 'Wr3', 'a3', 'b3')}
    del _L0_gnn_all

    def _L1_gnn_setup():
        import jax, jax.numpy as jnp
        import numpy as np
        N_NODES = 3125
        N_EDGES = 62500
        IN_SIZE = 64
        OUT_SIZE = 64
        EDGE_DIM = 16
        BN_EPS = 1e-05
        GIN_EPS = 0.0
        key = jax.random.key(seed)
        ks = jax.random.split(key, 10)
        s = 1.0 / np.sqrt(IN_SIZE)
        return {'x': jax.random.normal(ks[0], (N_NODES, IN_SIZE), dtype=jnp.float32), 'edge_index': jax.random.randint(ks[1], (2, N_EDGES), 0, N_NODES, dtype=jnp.int64), 'edge_attr': jax.random.normal(ks[2], (N_EDGES, EDGE_DIM), dtype=jnp.float32), 'W_edge': jax.random.uniform(ks[3], (IN_SIZE, EDGE_DIM), jnp.float32, -s, s), 'b_edge': jnp.zeros((IN_SIZE,), jnp.float32), 'W1': jax.random.uniform(ks[4], (OUT_SIZE, IN_SIZE), jnp.float32, -s, s), 'b1': jnp.zeros((OUT_SIZE,), jnp.float32), 'gamma': jnp.ones((OUT_SIZE,), jnp.float32), 'beta': jnp.zeros((OUT_SIZE,), jnp.float32), 'W2': jax.random.uniform(ks[5], (OUT_SIZE, OUT_SIZE), jnp.float32, -1.0 / np.sqrt(OUT_SIZE), 1.0 / np.sqrt(OUT_SIZE)), 'b2': jnp.zeros((OUT_SIZE,), jnp.float32)}
    _L1_gnn_all = _L1_gnn_setup()
    _L1_gnn_in = {k: v for k, v in _L1_gnn_all.items() if k in ('W_edge', 'b_edge', 'W1', 'b1', 'gamma', 'beta', 'W2', 'b2')}
    del _L1_gnn_all
    return {'x': x, 'src': src, 'dst': dst, 'edge_attr_16': edge_attr_16, 'L0_gnn_Wl1': _L0_gnn_in['Wl1'], 'L0_gnn_Wr1': _L0_gnn_in['Wr1'], 'L0_gnn_a1': _L0_gnn_in['a1'], 'L0_gnn_b1': _L0_gnn_in['b1'], 'L0_gnn_Wl2': _L0_gnn_in['Wl2'], 'L0_gnn_Wr2': _L0_gnn_in['Wr2'], 'L0_gnn_a2': _L0_gnn_in['a2'], 'L0_gnn_b2': _L0_gnn_in['b2'], 'L0_gnn_Wl3': _L0_gnn_in['Wl3'], 'L0_gnn_Wr3': _L0_gnn_in['Wr3'], 'L0_gnn_a3': _L0_gnn_in['a3'], 'L0_gnn_b3': _L0_gnn_in['b3'], 'L1_gnn_W_edge': _L1_gnn_in['W_edge'], 'L1_gnn_b_edge': _L1_gnn_in['b_edge'], 'L1_gnn_W1': _L1_gnn_in['W1'], 'L1_gnn_b1': _L1_gnn_in['b1'], 'L1_gnn_gamma': _L1_gnn_in['gamma'], 'L1_gnn_beta': _L1_gnn_in['beta'], 'L1_gnn_W2': _L1_gnn_in['W2'], 'L1_gnn_b2': _L1_gnn_in['b2']}

def reference(x, src, dst, edge_attr_16, L0_gnn_Wl1, L0_gnn_Wr1, L0_gnn_a1, L0_gnn_b1, L0_gnn_Wl2, L0_gnn_Wr2, L0_gnn_a2, L0_gnn_b2, L0_gnn_Wl3, L0_gnn_Wr3, L0_gnn_a3, L0_gnn_b3, L1_gnn_W_edge, L1_gnn_b_edge, L1_gnn_W1, L1_gnn_b1, L1_gnn_gamma, L1_gnn_beta, L1_gnn_W2, L1_gnn_b2):
    import jax
    import jax.numpy as jnp

    def _L0_gnn_ref(x, edge_index, Wl1, Wr1, a1, b1, Wl2, Wr2, a2, b2, Wl3, Wr3, a3, b3):
        import jax, jax.numpy as jnp
        import numpy as np
        N = 6250
        E = 62500
        C = 64
        H = 4
        O = C // H
        NEG_SLOPE = 0.2

        def _gatv2_layer(x, src, dst, Wl, Wr, a, b):
            xl = (x @ Wl).reshape(N, H, O)
            xr = (x @ Wr).reshape(N, H, O)
            s = jax.nn.leaky_relu(xl[src] + xr[dst], NEG_SLOPE)
            e = jnp.einsum('eho,ho->eh', s, a)
            m = jax.ops.segment_max(e, dst, num_segments=N)
            ex = jnp.exp(e - m[dst])
            denom = jax.ops.segment_sum(ex, dst, num_segments=N)
            alpha = ex / (denom[dst] + 1e-16)
            out = jax.ops.segment_sum(xl[src] * alpha[:, :, None], dst, num_segments=N)
            return out.reshape(N, H * O) + b
        src, dst = (edge_index[0], edge_index[1])
        h = jax.nn.relu(_gatv2_layer(x, src, dst, Wl1, Wr1, a1, b1))
        h = jax.nn.relu(_gatv2_layer(h, src, dst, Wl2, Wr2, a2, b2))
        h = _gatv2_layer(h, src, dst, Wl3, Wr3, a3, b3)
        return h

    def _L1_gnn_ref(x, edge_index, edge_attr, W_edge, b_edge, W1, b1, gamma, beta, W2, b2):
        import jax, jax.numpy as jnp
        import numpy as np
        N_NODES = 3125
        N_EDGES = 62500
        IN_SIZE = 64
        OUT_SIZE = 64
        EDGE_DIM = 16
        BN_EPS = 1e-05
        GIN_EPS = 0.0
        src = edge_index[0]
        dst = edge_index[1]
        ea = edge_attr @ W_edge.T + b_edge
        msg = jax.nn.relu(x[src] + ea)
        agg = jax.ops.segment_sum(msg, dst, num_segments=x.shape[0])
        h = (1.0 + GIN_EPS) * x + agg
        h = h @ W1.T + b1
        mean = jnp.mean(h, axis=0)
        var = jnp.var(h, axis=0)
        h = gamma * (h - mean) * jax.lax.rsqrt(var + BN_EPS) + beta
        h = jax.nn.relu(h)
        return h @ W2.T + b2
    edge_index = jnp.stack([src, dst])
    h = jnp.maximum(_layernorm(x, axis=-1), 0.0)
    x = x + _L0_gnn_ref(h, edge_index, L0_gnn_Wl1, L0_gnn_Wr1, L0_gnn_a1, L0_gnn_b1, L0_gnn_Wl2, L0_gnn_Wr2, L0_gnn_a2, L0_gnn_b2, L0_gnn_Wl3, L0_gnn_Wr3, L0_gnn_a3, L0_gnn_b3)
    h = jnp.maximum(_layernorm(x, axis=-1), 0.0)
    x = x + _L1_gnn_ref(h, edge_index, edge_attr_16, L1_gnn_W_edge, L1_gnn_b_edge, L1_gnn_W1, L1_gnn_b1, L1_gnn_gamma, L1_gnn_beta, L1_gnn_W2, L1_gnn_b2)
    return x

_drawn_inputs = setup_inputs


def setup_inputs(seed=0):
    import zlib

    import numpy as np

    out = dict(_drawn_inputs(seed))
    spreads = {'L0_gnn_b1': (0.0, 0.1),
     'L0_gnn_b2': (0.0, 0.1),
     'L0_gnn_b3': (0.0, 0.1),
     'L1_gnn_b_edge': (0.0, 0.1),
     'L1_gnn_b1': (0.0, 2.0),
     'L1_gnn_gamma': (1.0, 0.2),
     'L1_gnn_beta': (0.0, 0.1),
     'L1_gnn_b2': (0.0, 0.1)}
    factors = {'L0_gnn_Wr1': 200.0,
     'L0_gnn_a1': 2.777,
     'L0_gnn_Wr2': 200.0,
     'L0_gnn_a2': 64.0,
     'L0_gnn_Wr3': 200.0,
     'L0_gnn_a3': 200.0}
    for name, (base, spread) in spreads.items():
        noise = np.random.default_rng([zlib.crc32(name.encode()), seed]).standard_normal(out[name].shape)
        drawn = base * np.exp(spread * noise) if base else spread * noise
        out[name] = jnp.asarray(drawn.astype(out[name].dtype))
    for name, factor in factors.items():
        out[name] = (out[name] * factor).astype(out[name].dtype)
    return out
```

```python
from contextlib import ExitStack

import numpy as np

import concourse.bass as bass
from concourse import mybir

ALU = mybir.AluOpType
ACT = mybir.ActivationFunctionType
AX = mybir.AxisListType
F32 = mybir.dt.float32
BF16 = mybir.dt.bfloat16
I16 = mybir.dt.int16
I32 = mybir.dt.int32

P = 128
N, C, H, O = 6250, 64, 4, 16
E, KE = 200000, 16
LAYERS = 3
G = 16
J = 1568
TURNS = J // G
PAIRS = TURNS // 2
GE = 3
GD = G - GE
EP = P * J
B = 49
NB = P * B
GB = 7
GROUPS = B // GB
EC = GE * P
ROUND = 1.5 * 2.0 ** 23
G1 = G + 1
HO = O + 1
V = H * HO
ROW = V + H
SR = 196
SROWS = EP // SR
ZERO_ROW = EP
NEG = -1.0e38
EPS = 1e-5
SLOPE = 0.2
LAST_PAD = N - (P - 1) * B


def build(nc, t):
    with ExitStack() as ctx:
        def sb(name, shape, dt=F32):
            return ctx.enter_context(nc.sbuf_tensor("sb_" + name, shape, dt))

        def sem(name):
            return ctx.enter_context(nc.semaphore(name))

        def two(name):
            return [sem(f"{name}{k}") for k in range(2)]

        xl_table = nc.dram_tensor("xl_table", (NB, C), F32, kind="Internal").ap()
        xr_table = nc.dram_tensor("xr_table", (NB, C), F32, kind="Internal").ap()
        marks = nc.dram_tensor("marks", (EP + NB, C), F32, kind="Internal").ap()
        state_rows = nc.dram_tensor("state_rows", (EP + 1 + P, ROW), F32, kind="Internal").ap()
        agg_rows = nc.dram_tensor("agg_rows", (EP + 1 + P, C), F32, kind="Internal").ap()
        splitters = nc.dram_tensor("splitters", (SROWS,), I32, kind="Internal").ap()
        ranks = nc.dram_tensor("ranks", (1 + NB,), I32, kind="Internal").ap()
        codes = nc.dram_tensor("codes", (TURNS + 2, EC), I16, kind="Internal").ap()
        marks_runs = marks[0:EP, :].rearrange("(p j) c -> p (j c)", p=P)
        state_runs = state_rows[0:EP, :].rearrange("(p j) c -> p (j c)", p=P)
        agg_runs = agg_rows[0:EP, :].rearrange("(p j) c -> p (j c)", p=P)

        x = sb("x", [P, B, C])
        h = sb("h", [P, B, C])
        XL = sb("XL", [P, B, C])
        XR = sb("XR", [P, B, C])
        node_rows = sb("node_rows", [P, B, ROW])
        recip = sb("recip", [P, B, H])
        stat = sb("stat", [P, 4, B])
        ranks_f = sb("ranks_f", [P, 4, B])
        ranks_i = sb("ranks_i", [P, 2, B], I32)
        search_row = sb("search_row", [P, B], I32)
        last_edge = sb("last_edge", [P, B], I32)
        first_edge = sb("first_edge", [P, B], I32)
        wide = sb("wide", [P, 2 * NB + 256])
        searched = wide[:, 0:B * SR].rearrange("p (b r) -> p b r", b=B)
        searched_i = searched.bitcast(I32)
        dst_i = wide[:, B * SR:B * SR + J].bitcast(I32)
        dst_before_i = wide[:, B * SR + J:B * SR + 2 * J].bitcast(I32)
        split_s = sb("split_s", [P, SROWS // P], I32)
        split_all = XR[:].rearrange("p b c -> p (b c)")[:, 0:SROWS].bitcast(I32)
        split_hit = XR[:].rearrange("p b c -> p (b c)")[:, SROWS:2 * SROWS]
        part_words = B * C // 2
        xl_part = [wide[:, k * part_words:(k + 1) * part_words].bitcast(BF16) for k in range(3)]
        at = 3 * part_words
        one_hot = [wide[:, at + k * GB * EC // 2:at + (k + 1) * GB * EC // 2].bitcast(BF16).rearrange("p (m e) -> p m e", m=GB)
                   for k in range(2)]
        at += GB * EC
        code = [wide[:, at + k * EC // 2:at + (k + 1) * EC // 2].bitcast(I16) for k in range(2)]
        at += EC
        left = wide[:, at:at + 2 * GB * C].rearrange("p (a n) -> p a n", a=2)
        at += 2 * GB * C
        attr = wide[:, at:at + 4 * P].rearrange("p (k e) -> p k e", k=2)
        ident = sb("ident", [P, P])
        node_no = sb("node_no", [P, B])
        code_no = sb("code_no", [P, GB])
        pick_no = sb("pick_no", [P, GB])
        src_r = sb("src_r", [P, TURNS, GE])
        pick = sb("pick", [P, GB, GE], I32)
        run_no = sb("run_no", [P, 2])
        w_gat = sb("w_gat", [C, LAYERS * 2 * C])
        a_all = sb("a_all", [P, LAYERS * C])
        b_all = sb("b_all", [P, LAYERS * C])
        floor_all = sb("floor_all", [P, LAYERS])
        w_blk = sb("w_blk", [P, 8 * C])
        w1t = sb("w1t", [C, C])
        w2t = sb("w2t", [C, C])
        cols = sb("cols", [C, 4])
        be_all = sb("be_all", [P, C])
        b2_all = sb("b2_all", [P, C])
        same = sb("same", [P, TURNS, G1])
        neg = sb("neg", [P, TURNS, G1])
        run_f = sb("run_f", [P, 8])
        run_first = sb("run_first", [P, 1], I32)
        run_next = sb("run_next", [P, 1], I32)
        run_row = sb("run_row", [P, 1], I32)
        mend_row = sb("mend_row", [P, 1], I32)
        cont_in = sb("cont_in", [P, 2, P])
        cont = sb("cont", [P, P])
        cont_neg = sb("cont_neg", [P, P])
        xr_first = sb("xr_first", [P, C])
        fin_s = sb("fin_s", [P, V])
        fin_m = sb("fin_m", [P, H, HO])
        rm = sb("rm", [P, P + 1])
        rs = sb("rs", [P, P + 1])
        rf = sb("rf", [P, P])
        rt = sb("rt", [P, P])
        ra = sb("ra", [P, 2, P])
        local = sb("local", [P, ROW])
        mend = sb("mend", [P, ROW])
        mm = sb("mm", [P, H, HO])
        mw = sb("mw", [P, 2, V])
        carry_in = sb("carry_in", [P, 2, V])
        idx = sb("idx", [P, 2, G], I32)
        xl = sb("xl", [P, 2, G, C])
        mark = sb("mark", [P, 2, G, C])
        xr_in = sb("xr_in", [P, C, G1])
        xr_out = sb("xr_out", [P, C, G1])
        same_c = sb("same_c", [P, C, G1])
        neg_h = sb("neg_h", [P, H, G1])
        s = sb("s", [P, G, C])
        lr = sb("lr", [P, G, C])
        e_in = sb("e_in", [P, H, G1])
        m_run = sb("m_run", [P, H, G1])
        w_arg = sb("w_arg", [P, H, G])
        f_arg = sb("f_arg", [P, H, G])
        f_h = sb("f_h", [P, H, G1])
        f_all = sb("f_all", [P, V, G1])
        v_in = sb("v_in", [P, V, G1])
        s_run = sb("s_run", [P, V, G1])
        turn_out = sb("turn_out", [P, 2, G, ROW])

        pe_src = s[0:TURNS].rearrange("p g c -> p (g c)")[:, 0:EC].bitcast(I32)
        pe_tmp = s[0:TURNS].rearrange("p g c -> p (g c)")[:, EC:2 * EC]
        pe_code = lr[0:TURNS].rearrange("p g c -> p (g c)")[:, 0:EC // 2].bitcast(I16)
        pe_src_r = lr[:].rearrange("p g c -> p (g c)")[:, EC:EC + TURNS * GE].bitcast(I32)
        src_r_flat = src_r[:].rearrange("p n a -> p (n a)")
        v_heads = v_in[:].rearrange("p (h o) g -> p h o g", h=H)
        v_lin = v_in[:, 0:C, :]
        lin_run = s_run[:, 0:C, :]
        zT = wide[0:C, 0:NB]
        uT = wide[0:C, NB:2 * NB]

        pG = ctx.enter_context(nc.psum_tensor("pG", [P, 2 * GE, 512], F32))
        pT, pP = pG[:, 0:2, :], pG[:, 2:4, :]
        pE = ctx.enter_context(nc.psum_tensor("pE", [P, 1024], F32))

        hT = xl[0:C, 0].rearrange("p g c -> p (g c)")[:, 0:GB * P].rearrange("p (i q) -> p i q", i=GB)
        bn = sb("bn", [C, 8])

        s_x, s_const, s_dst, s_weights = sem("x_in"), sem("constants_in"), sem("dst_in"), sem("weights_in")
        s_zero, s_filled, s_wblk0 = sem("zeros_ready"), sem("tables_zeroed"), sem("w_blk_zeroed")
        s_wblk = sem("w_blk_in")
        s_pro = sem("dve_prologue_steps")
        s_std = sem("std_ready")
        s_split, s_split_out, s_split_in = sem("splitters_cut"), sem("splitters_out"), sem("splitters_in")
        s_srow = sem("search_rows_found")
        s_searched = [sem(f"searched{g}") for g in range(GROUPS)]
        s_rank, s_rank_out, s_rank_in = sem("ranks_ready"), sem("ranks_out"), sem("ranks_in")
        s_index, s_masks = sem("node_edges_known"), sem("masks_ready")
        s_contT = sem("cont_turned")
        s_h = sem("h_ready")
        s_hT, s_hTc, s_pp, s_xlxr = sem("h_turned"), sem("hT_copied"), sem("xlxr_product"), sem("xlxr_copied")
        s_tab_l, s_tab_r = sem("xl_table_out"), sem("xr_table_out")
        s_marked, s_xr_first = sem("marks_scattered"), sem("xr_first_in")
        s_start = sem("runs_started")
        s_src, s_code_cut, s_code_out = sem("pe_sources_in"), sem("codes_cut"), sem("codes_out")
        s_code, s_hot, s_pg, s_picked = two("code_in"), two("one_hot_ready"), two("pe_gathered"), two("pe_rows_picked")
        s_parts = sem("xl_parts_ready")
        s_part_steps, s_pick = sem("dve_part_steps"), sem("dve_pick_steps")
        s_idx, s_mark, s_xl = two("idx_in"), two("mark_in"), two("xl_gathered")
        s_passed = sem("waits_passed")
        s_xrin, s_same, s_neg = sem("xr_in_ready"), sem("same_spread"), sem("neg_spread")
        s_turned, s_used = two("mark_turned"), two("xl_used")
        s_xr, s_warg, s_farg = sem("xr_scanned"), sem("w_arg_ready"), sem("f_arg_ready")
        s_w, s_fh, s_f = sem("w_ready"), sem("f_h_ready"), sem("f_spread")
        s_sums, s_out, s_stored = sem("sums_scanned"), sem("turn_out_ready"), two("turn_stored")
        s_turn = sem("dve_turn_steps")
        s_fin, s_finT = sem("run_ends_ready"), sem("run_ends_turned")
        s_rarg, s_rexp, s_rsc, s_rback = sem("run_args"), sem("run_exps"), sem("run_scans"), sem("run_carries_back")
        s_local, s_marg, s_mexp = sem("local_in"), sem("mend_args"), sem("mend_exps")
        s_mend, s_mended = sem("mend_ready"), sem("rows_mended")
        s_ends = sem("dve_run_end_steps")
        s_nrow = [sem(f"node_rows_in{g}") for g in range(GROUPS)]
        s_node = sem("dve_node_steps")
        s_attr, s_ea, s_ea_used = two("attr_in"), two("ea_ready"), sem("ea_used")
        s_lin, s_lin_relu = sem("lin_sum_ready"), sem("lin_relu_ready")
        s_gin = sem("dve_gin_steps")
        s_z, s_zT, s_zTc = sem("z_ready"), sem("z_turned"), sem("zT_copied")
        s_u, s_uc, s_sq, s_bnstd, s_bnp, s_y = (sem(n) for n in (
            "u_product", "u_copied", "u_squared", "bn_std_ready", "bn_params", "y_ready"))
        s_o, s_final, s_result = sem("o_product"), sem("final_ready"), sem("result_out")

        def chain(eng, signal, base=0):
            count = [0]

            def done(ins):
                count[0] += 1
                ins.then_inc(signal, 1)

            def last():
                eng.wait_ge(signal, base + count[0])

            return done, last, count

        K_TURN, K_ENDS, K_NODE, K_LIN = 9, 11, 4 * GROUPS, 3

        block = ctx.enter_context(nc.Block())

        @block.sync
        def _(sp):
            sp.dma_start(dst_i, t["dst_edges"]).then_inc(s_dst, 16)
            sp.dma_start(dst_before_i, t["dst_before"]).then_inc(s_dst, 16)
            sp.dma_start(run_next[:, :], t["dst_next_run"]).then_inc(s_dst, 16)
            sp.dma_start(x[:].rearrange("p b c -> p (b c)"), t["x_nodes"].rearrange("(p b) c -> p (b c)", p=P)).then_inc(s_x, 16)
            sp.dma_start(ident[:, :], t["identity"]).then_inc(s_const, 16)
            sp.dma_start(node_no[:, :], t["node_no"]).then_inc(s_const, 16)
            sp.dma_start(run_no[:, :], t["run_no"]).then_inc(s_const, 16)
            sp.dma_start(code_no[:, :], t["code_no"]).then_inc(s_const, 16)
            sp.dma_start(pick_no[:, :], t["pick_no"]).then_inc(s_const, 16)
            sp.dma_start(pe_src, t["src_pe_places"]).then_inc(s_src, 16)
            sp.dma_start(pe_src_r, t["src_pe_edges"]).then_inc(s_src, 16)
            sp.wait_ge(s_split, 1)
            sp.dma_start(splitters.rearrange("(p k) -> p k", p=P), split_s[:, :]).then_inc(s_split_out, 16)
            sp.wait_ge(s_split_out, 16)
            sp.dma_start(split_all, splitters.partition_broadcast(P)).then_inc(s_split_in, 16)
            sp.dma_start(w_gat[:, :], t["w_gat"]).then_inc(s_weights, 16)
            sp.dma_start(a_all[:, :], t["a_rows"].partition_broadcast(P)).then_inc(s_weights, 16)
            sp.dma_start(b_all[:, :], t["b_rows"].partition_broadcast(P)).then_inc(s_weights, 16)
            sp.dma_start(w1t[:, :], t["w1_t"]).then_inc(s_weights, 16)
            sp.dma_start(w2t[:, :], t["w2_t"]).then_inc(s_weights, 16)
            sp.dma_start(cols[:, 0:3], t["channel_cols"]).then_inc(s_weights, 16)
            sp.dma_start(be_all[:, :], t["b_edge"].partition_broadcast(P)).then_inc(s_weights, 16)
            sp.dma_start(b2_all[:, :], t["b2"].partition_broadcast(P)).then_inc(s_weights, 16)
            sp.wait_ge(s_wblk0, 1)
            for g in range(8):
                sp.dma_start(w_blk[g * KE:(g + 1) * KE, g * C:(g + 1) * C], t["w_edge_t"]).then_inc(s_wblk, 16)
            sp.wait_ge(s_zero, 1)
            zeros = node_rows[:].rearrange("p b c -> p (b c)")
            for table in (state_rows, agg_rows):
                width = table.shape[1]
                sp.dma_start(table[ZERO_ROW:ZERO_ROW + 1, :], zeros[0:1, 0:width]).then_inc(s_filled, 16)
                sp.dma_start(table[ZERO_ROW + 1:ZERO_ROW + 1 + P, :], zeros[:, 0:width]).then_inc(s_filled, 16)
            with sp.Fori(0, J * C // (B * C)) as i:
                sp.dma_start(marks_runs[:, bass.ds(i * (B * C), B * C)], zeros[:, 0:B * C]).then_inc(s_filled, 16)
            sp.wait_ge(s_rank, 1)
            sp.dma_start(ranks[0:1].unsqueeze(0), ranks_i[0:1, 1, 0:1]).then_inc(s_rank_out, 16)
            sp.dma_start(ranks[1:1 + NB].rearrange("(p b) -> p b", p=P), ranks_i[:, 0, :]).then_inc(s_rank_out, 16)
            sp.wait_ge(s_rank_out, 32)
            sp.dma_start(ranks_i[:, 1, :], ranks[0:NB].rearrange("(p b) -> p b", p=P)).then_inc(s_rank_in, 16)

            sp.wait_ge(s_code_cut, 1)
            sp.dma_start(codes[0:TURNS, :], pe_code).then_inc(s_code_out, 16)
            sp.dma_start(codes[TURNS:TURNS + 2, :], pe_code[0:2, :]).then_inc(s_code_out, 16)
            sp.wait_ge(s_code_out, 32)
            sp.wait_ge(s_index, 1)
            for k in range(2):
                sp.dma_start(code[k], codes[k, :].partition_broadcast(P)).then_inc(s_code[k], 16)

            def turn_loads(use, turn, k, marked):
                sp.wait_ge(s_hot[k], use + 1)
                sp.dma_start(code[k], codes[bass.ds(turn + 2, 1), :].rearrange("a e -> (a e)").partition_broadcast(P)
                             ).then_inc(s_code[k], 16)
                sp.wait_ge(s_xl[k], use * (16 * GD))
                sp.dma_start(idx[:, k, :], t["src_edges"][:, bass.ds(turn * G, G)]).then_inc(s_idx[k], 16)
                if marked:
                    sp.wait_ge(s_turned[k], use)
                    sp.dma_start(mark[:, k].rearrange("p g c -> p (g c)"),
                                 marks_runs[:, bass.ds(turn * (G * C), G * C)]).then_inc(s_mark[k], 16)
                else:
                    sp.wait_ge(s_ea[k], use - LAYERS * PAIRS)
                    sp.dma_start(attr[:, k, :], t["attr_t"][bass.ds(turn, 1)].rearrange("a p q -> (a p) q")).then_inc(s_attr[k], 16)

            with sp.Fori(0, LAYERS) as l:
                sp.wait_ge(s_xlxr, (l + 1) * GROUPS)
                sp.dma_start(xl_table.rearrange("(p b) c -> p (b c)", p=P), XL[:].rearrange("p b c -> p (b c)")).then_inc(s_tab_l, 16)
                sp.dma_start(xr_table.rearrange("(p b) c -> p (b c)", p=P), XR[:].rearrange("p b c -> p (b c)")).then_inc(s_tab_r, 16)
                sp.wait_ge(s_marked, (l + 1) * (16 * B))
                sp.sem_inc(s_passed, 1)
                with sp.Fori(0, PAIRS) as i:
                    for k in range(2):
                        turn_loads(l * PAIRS + i, 2 * i + k, k, True)
            sp.wait_ge(s_gin, K_LIN)
            sp.dma_start(xl_table.rearrange("(p b) c -> p (b c)", p=P), XL[:].rearrange("p b c -> p (b c)")).then_inc(s_tab_l, 16)
            with sp.Fori(0, PAIRS) as i:
                for k in range(2):
                    turn_loads(i + LAYERS * PAIRS, 2 * i + k, k, False)
            result = t["out"].rearrange("(p b) c -> p b c", p=P)
            for g in range(GROUPS):
                sl = slice(g * GB, (g + 1) * GB)
                sp.wait_ge(s_final, g + 1)
                sp.dma_start(result[:, sl, :], XR[:, sl, :]).then_inc(s_result, 16)
            sp.wait_ge(s_result, 16 * GROUPS)

        @block.gpsimd
        def _(pool):
            def gather(dst, table, index):
                return pool.indirect_dma_start(out=dst, out_offset=None, in_=table,
                                               in_offset=bass.IndirectOffsetOnAxis(ap=index, axis=0))

            def scatter(table, index, src):
                return pool.indirect_dma_start(out=table, out_offset=bass.IndirectOffsetOnAxis(ap=index, axis=0),
                                               in_=src, in_offset=None)

            for g in range(GROUPS):
                pool.wait_ge(s_srow, g + 1)
                for b in range(g * GB, (g + 1) * GB):
                    gather(searched_i[:, b, :], t["dst_rows"], search_row[:, b:b + 1]).then_inc(s_searched[g], 16)
            pool.wait_ge(s_filled, 16 * (4 + J // B))
            pool.wait_ge(s_index, 1)

            def turn_gathers(use, k):
                pool.wait_ge(s_used[k], use)
                pool.wait_ge(s_idx[k], (use + 1) * 16)
                pool.sem_inc(s_passed, 1)
                for j in range(GD):
                    gather(xl[:, k, j, :], xl_table, idx[:, k, j:j + 1]).then_inc(s_xl[k], 16)

            with pool.Fori(0, LAYERS) as l:
                for g in range(GROUPS):
                    pool.wait_ge(s_xlxr, l * GROUPS + (g + 1))
                    pool.sem_inc(s_passed, 1)
                    for b in range(g * GB, (g + 1) * GB):
                        scatter(marks, first_edge[:, b:b + 1], XR[:, b, :]).then_inc(s_marked, 16)
                pool.wait_ge(s_tab_r, (l + 1) * 16)
                pool.wait_ge(s_tab_l, (l + 1) * 16)
                pool.sem_inc(s_passed, 1)
                gather(xr_first[:, :], xr_table, run_first[:, 0:1]).then_inc(s_xr_first, 16)
                with pool.Fori(0, PAIRS) as i:
                    for k in range(2):
                        turn_gathers(l * PAIRS + i, k)
                pool.wait_ge(s_stored[0], (l + 1) * (16 * PAIRS))
                pool.wait_ge(s_stored[1], (l + 1) * (16 * PAIRS))
                pool.sem_inc(s_passed, 1)
                gather(local[:, :], state_rows, run_row[:, 0:1]).then_inc(s_local, 16)
                pool.wait_ge(s_mend, l + 1)
                pool.sem_inc(s_passed, 1)
                scatter(state_rows, mend_row[:, 0:1], mend[:, :]).then_inc(s_mended, 16)
                pool.wait_ge(s_mended, (l + 1) * 16)
                pool.sem_inc(s_passed, 1)
                for g in range(GROUPS):
                    for b in range(g * GB, (g + 1) * GB):
                        gather(node_rows[:, b, :], state_rows, last_edge[:, b:b + 1]).then_inc(s_nrow[g], 16)
            pool.wait_ge(s_tab_l, (LAYERS + 1) * 16)
            with pool.Fori(0, PAIRS) as i:
                for k in range(2):
                    turn_gathers(i + LAYERS * PAIRS, k)
            pool.wait_ge(s_stored[0], (LAYERS + 1) * (16 * PAIRS))
            pool.wait_ge(s_stored[1], (LAYERS + 1) * (16 * PAIRS))
            gather(local[:, 0:C], agg_rows, run_row[:, 0:1]).then_inc(s_local, 16)
            pool.wait_ge(s_mend, LAYERS + 1)
            scatter(agg_rows, mend_row[:, 0:1], mend[:, 0:C]).then_inc(s_mended, 16)
            pool.wait_ge(s_mended, (LAYERS + 1) * 16)
            for g in range(GROUPS):
                for b in range(g * GB, (g + 1) * GB):
                    gather(node_rows[:, b, 0:C], agg_rows, last_edge[:, b:b + 1]).then_inc(s_nrow[g], 16)

        def place(psum, i):
            return psum[:, i // 4, (i % 4) * P:(i % 4 + 1) * P]

        @block.tensor
        def _(pe):
            pe.wait_ge(s_const, 80)
            pe.wait_ge(s_contT, 1)
            pe.transpose(pT[:, 0, 0:P], cont_in[:, 0, :], ident[:, :])
            pe.transpose(pT[:, 0, P:2 * P], cont_in[:, 1, :], ident[:, :]).then_inc(s_contT, 1)
            pe.wait_ge(s_weights, 16 * 8)
            pe.wait_ge(s_contT, 3)

            def pe_gather(use, k):
                pe.wait_ge(s_hot[k], use + 1)
                pe.wait_ge(s_picked[k], use)
                pe.sem_inc(s_passed, 1)
                for a in range(GE):
                    for m in range(GB):
                        for part in range(3):
                            product = pe.matmul(pG[:, k * GE + a, 0:GB * C], one_hot[k][:, m, a * P:(a + 1) * P],
                                                xl_part[part][:, m * GB * C:(m + 1) * GB * C],
                                                start=(m == 0 and part == 0), stop=(m == GB - 1 and part == 2))
                product.then_inc(s_pg[k], 1)

            with pe.Fori(0, LAYERS) as l:
                for g in range(GROUPS):
                    pe.wait_ge(s_h, l * GROUPS + (g + 1))
                    pe.wait_ge(s_hTc, l * GROUPS + g)
                    pe.sem_inc(s_passed, 1)
                    for i in range(GB):
                        product = pe.transpose(place(pT, i)[0:C, :], h[:, g * GB + i, :], ident[:, :])
                    product.then_inc(s_hT, 1)
                    pe.wait_ge(s_hTc, l * GROUPS + (g + 1))
                    pe.wait_ge(s_xlxr, l * GROUPS + g)
                    pe.sem_inc(s_passed, 1)
                    for i in range(GB):
                        product = pe.matmul(place(pP, i), hT[:, i, :], w_gat[:, bass.ds(l * (2 * C), 2 * C)], start=True, stop=True)
                    product.then_inc(s_pp, 1)
                pe.wait_ge(s_parts, (l + 1) * GROUPS)
                pe.sem_inc(s_passed, 1)
                with pe.Fori(0, PAIRS) as i:
                    for k in range(2):
                        pe_gather(l * PAIRS + i, k)
                pe.wait_ge(s_fin, l + 1)
                pe.sem_inc(s_passed, 1)
                pe.transpose(pT[0:V, 0, 0:P], fin_s[:, :], ident[:, :])
                pe.transpose(pT[0:V, 0, P:2 * P], fin_m[:].rearrange("p h o -> p (h o)"), ident[:, :]).then_inc(s_finT, 1)
                pe.wait_ge(s_rsc, l + 1)
                pe.sem_inc(s_passed, 1)
                pe.transpose(pP[:, 0, 0:V], rs[0:V, 0:P], ident[0:V, 0:V])
                pe.transpose(pP[:, 0, P:P + V], rm[0:V, 0:P], ident[0:V, 0:V]).then_inc(s_rback, 1)
            pe.wait_ge(s_wblk, 16 * 8)
            pe.wait_ge(s_parts, (LAYERS + 1) * GROUPS)
            pe.sem_inc(s_passed, 1)
            with pe.Fori(0, PAIRS) as i:
                for k in range(2):
                    pe_gather(i + LAYERS * PAIRS, k)
                    pe.wait_ge(s_attr[k], (i + 1) * 16)
                    pe.wait_ge(s_ea_used, 2 * i + k)
                    pe.sem_inc(s_passed, 1)
                    for q in range(2):
                        product = pe.matmul(pE[:, q * 512:(q + 1) * 512], attr[:, k, q * P:(q + 1) * P], w_blk[:, :],
                                        start=True, stop=True)
                    product.then_inc(s_ea[k], 1)
            pe.wait_ge(s_fin, LAYERS + 1)
            pe.transpose(pT[0:C, 0, 0:P], fin_s[:, 0:C], ident[:, :]).then_inc(s_finT, 1)
            pe.wait_ge(s_rsc, LAYERS + 1)
            pe.transpose(pP[:, 0, 0:C], rs[0:C, 0:P], ident[0:C, 0:C]).then_inc(s_rback, 1)
            for g in range(GROUPS):
                pe.wait_ge(s_z, g + 1)
                if g:
                    pe.wait_ge(s_zTc, g)
                for i in range(GB):
                    product = pe.transpose(place(pT, i)[0:C, :], h[:, g * GB + i, :], ident[:, :])
                product.then_inc(s_zT, 1)
            pe.wait_ge(s_zTc, GROUPS)
            for q in range(0, B, 4):
                n = min(4, B - q) * P
                k = (q // 4) % 2
                if q >= 8:
                    pe.wait_ge(s_uc, q // 4 - 1)
                pe.matmul(pP[0:C, k, 0:n], w1t[:, :], zT[:, q * P:q * P + n], start=True, stop=True).then_inc(s_u, 1)
            pe.wait_ge(s_y, 1)
            for g in range(GROUPS):
                if g:
                    pe.wait_ge(s_final, g)
                for i in range(GB):
                    b = g * GB + i
                    product = pe.matmul(pT[:, i // 4, (i % 4) * P:(i % 4) * P + C], zT[:, b * P:(b + 1) * P], w2t[:, :],
                                    start=True, stop=True)
                product.then_inc(s_o, 1)

        @block.scalar
        def _(act):
            def copy(out, in_):
                return act.activation(out, in_, ACT.Copy)

            act.wait_ge(s_std, 1)
            act.activation(stat[:, 2, :], stat[:, 1, :], ACT.Sqrt).then_inc(s_std, 1)

            def spread(turn_all, turn, width, use_neg):
                act.wait_ge(s_xr, turn_all)
                copy(same_c[:, :, :], same[:, bass.ds(turn, 1), :].to_broadcast([P, width, G1])).then_inc(s_same, 1)
                if use_neg:
                    act.wait_ge(s_farg, turn_all)
                    copy(neg_h[:, :, :], neg[:, bass.ds(turn, 1), :].to_broadcast([P, H, G1])).then_inc(s_neg, 1)

            def hand_out(all_before, stored, turn, k, table, rows, attention):
                act.wait_ge(s_sums, all_before)
                act.wait_ge(s_stored[k], stored)
                if attention:
                    copy(turn_out[:, k, :, V:ROW], m_run[:, :, 1:G1].rearrange("p h g -> p g h"))
                    copy(turn_out[:, k, :, 0:V], s_run[:, :, 1:G1].rearrange("p v g -> p g v")).then_inc(s_out, 1)
                    src = turn_out[:, k].rearrange("p g r -> p (g r)")
                else:
                    lin = turn_out[:, k].rearrange("p g r -> p (g r)")[:, 0:G * C]
                    copy(lin.rearrange("p (g c) -> p g c", g=G), lin_run[:, :, 1:G1].rearrange("p c g -> p g c")).then_inc(s_out, 1)
                    src = lin
                act.wait_ge(s_out, all_before)
                act.dma_start(table[:, bass.ds(turn * (G * rows), G * rows)], src).then_inc(s_stored[k], 16)

            def attention_turn(l, i, k, first=False):
                use = l * PAIRS + i
                turn = 2 * i + k
                turn_all = l * TURNS + 2 * i + k
                act.wait_ge(s_mark[k], (use + 1) * 16)
                act.wait_ge(s_xr, turn_all)
                copy(xr_in[:, :, 1:G1], mark[:, k].rearrange("p g c -> p c g")).then_inc(s_turned[k], 1)
                spread(turn_all, turn, C, True)
                if not first:
                    hand_out(turn_all, (use + k - 1) * 16, turn - 1, 1 - k, state_runs, ROW, True)
                act.wait_ge(s_warg, turn_all + 1)
                act.activation(v_heads[:, :, O, 1:G1], w_arg[:, :, :], ACT.Exp).then_inc(s_w, 1)
                act.wait_ge(s_farg, turn_all + 1)
                act.activation(f_h[:, :, 1:G1], f_arg[:, :, :], ACT.Exp).then_inc(s_fh, 1)
                act.wait_ge(s_fh, turn_all + 1)
                copy(f_all[:].rearrange("p (h o) g -> p h o g", h=H), f_h[:].unsqueeze(2).to_broadcast([P, H, HO, G1])).then_inc(s_f, 1)

            with act.Fori(0, LAYERS) as l:
                for g in range(GROUPS):
                    act.wait_ge(s_hT, l * GROUPS + (g + 1))
                    copy(hT[:, 0:4, :], pT[0:C, 0, :].rearrange("p (i q) -> p i q", i=4))
                    copy(hT[:, 4:GB, :], pT[0:C, 1, 0:3 * P].rearrange("p (i q) -> p i q", i=3)).then_inc(s_hTc, 1)
                    act.wait_ge(s_pp, l * GROUPS + (g + 1))
                    for half, (lo, n) in enumerate(((0, 4), (4, 3))):
                        both = pP[:, half, 0:n * P].rearrange("p (i q) -> p i q", i=n)
                        copy(XL[:, g * GB + lo:g * GB + lo + n, :], both[:, :, 0:C])
                        last_ = copy(XR[:, g * GB + lo:g * GB + lo + n, :], both[:, :, C:2 * C])
                    last_.then_inc(s_xlxr, 1)
                act.wait_ge(s_masks, 1)
                act.wait_ge(s_start, l + 1)
                attention_turn(l, 0, 0, first=True)
                attention_turn(l, 0, 1)
                with act.Fori(1, PAIRS) as i:
                    for k in range(2):
                        attention_turn(l, i, k)
                hand_out((l + 1) * TURNS, (l + 1) * (16 * PAIRS) - 16, TURNS - 1, 1, state_runs, ROW, True)
                act.wait_ge(s_rarg, l + 1)
                act.activation(rf[0:V, :], ra[0:V, 0, :], ACT.Exp)
                act.activation(rt[0:V, :], ra[0:V, 1, :], ACT.Exp).then_inc(s_rexp, 1)
                act.wait_ge(s_marg, l + 1)
                act.activation(mw[:, :, :], mw[:, :, :], ACT.Exp).then_inc(s_mexp, 1)

            act.wait_ge(s_std, 3)
            act.activation(stat[:, 2, :], stat[:, 1, :], ACT.Sqrt).then_inc(s_std, 1)

            def linear_turn(i, k, first=False):
                use = i + LAYERS * PAIRS
                turn = 2 * i + k
                turn_all = 2 * i + (k + LAYERS * TURNS)
                spread_same = same[:, bass.ds(turn, 1), :].to_broadcast([P, C, G1])
                act.wait_ge(s_sums, turn_all)
                copy(same_c[:, :, :], spread_same).then_inc(s_same, 1)
                act.wait_ge(s_lin, turn + 1)
                act.activation(v_lin[:, :, 1:G1], s[:].rearrange("p g c -> p c g"), ACT.Relu).then_inc(s_lin_relu, 1)
                if not first:
                    hand_out(turn_all, (use + k - 1) * 16, turn - 1, 1 - k, agg_runs, C, False)

            act.wait_ge(s_gin, K_LIN + 1)
            linear_turn(0, 0, first=True)
            linear_turn(0, 1)
            with act.Fori(1, PAIRS) as i:
                for k in range(2):
                    linear_turn(i, k)
            hand_out((LAYERS + 1) * TURNS, (LAYERS + 1) * (16 * PAIRS) - 16, TURNS - 1, 1, agg_runs, C, False)

            for g in range(GROUPS):
                act.wait_ge(s_zT, g + 1)
                copy(zT[:, g * GB * P:(g * GB + 4) * P], pT[0:C, 0, :])
                copy(zT[:, (g * GB + 4) * P:(g + 1) * GB * P], pT[0:C, 1, 0:3 * P]).then_inc(s_zTc, 1)
            for q in range(0, B, 4):
                n = min(4, B - q) * P
                act.wait_ge(s_u, q // 4 + 1)
                act.activation(uT[:, q * P:q * P + n], pP[0:C, (q // 4) % 2, 0:n], ACT.Identity, bias=cols[:, 0:1]).then_inc(s_uc, 1)
            act.wait_ge(s_sq, 1)
            act.activation(zT, uT, ACT.Square).then_inc(s_sq, 1)
            act.wait_ge(s_bnstd, 1)
            act.activation(bn[:, 5:6], bn[:, 4:5], ACT.Sqrt).then_inc(s_bnstd, 1)
            act.wait_ge(s_bnp, 1)
            act.activation(zT, uT, ACT.Relu, bias=cols[:, 2:3], scale=bn[:, 7:8]).then_inc(s_y, 1)

        @block.vector
        def _(dve):
            tt, ts, cp, red = dve.tensor_tensor, dve.tensor_scalar, dve.tensor_copy, dve.tensor_reduce

            def over(ap, n):
                return ap.unsqueeze(len(ap.shape)).to_broadcast(list(ap.shape) + [n])

            def blocks(ap, n):
                return ap.unsqueeze(1).to_broadcast([P, n] + list(ap.shape[1:]))

            done, last, steps = chain(dve, s_pro)

            def layernorm(dst, src, std_before, done, last):
                done(red(stat[:, 0, :], src, AX.X, ALU.add)); last()
                done(ts(stat[:, 0, :], stat[:, 0, :], 1.0 / C, None, ALU.mult)); last()
                done(tt(XL[:], src, over(stat[:, 0, :], C), ALU.subtract)); last()
                done(tt(dst, XL[:], XL[:], ALU.mult)); last()
                done(red(stat[:, 1, :], dst, AX.X, ALU.add)); last()
                ts(stat[:, 1, :], stat[:, 1, :], 1.0 / C, EPS, ALU.mult, ALU.add).then_inc(s_std, 1)
                dve.wait_ge(s_std, std_before + 2)
                done(dve.reciprocal(stat[:, 3, :], stat[:, 2, :])); last()
                done(tt(dst, XL[:], over(stat[:, 3, :], C), ALU.mult)); last()

            dve.memset(node_rows[:], 0.0).then_inc(s_zero, 1)
            dve.memset(w_blk[:], 0.0).then_inc(s_wblk0, 1)
            dve.memset(f_h[:], 0.0)
            dve.memset(same[:, :, 0:1], 0.0)
            dve.memset(neg[:, :, 0:1], NEG)
            dve.memset(rs[:], 0.0)
            dve.memset(rm[:], NEG)
            dve.memset(floor_all[:, 0:LAYERS - 1], 0.0)
            dve.memset(floor_all[:, LAYERS - 1:LAYERS], -3.0e38)
            done(dve.memset(ranks_f[:, 3, :], 0.0)); last()
            dve.wait_ge(s_dst, 48)
            cp(split_s[:, :], dst_i.rearrange("p (k r) -> p k r", r=SR)[:, :, SR - 1]).then_inc(s_split, 1)
            grid = "p (n g) -> p n g"
            done(tt(same[:, :, 1:G1], dst_i.rearrange(grid, g=G), dst_before_i.rearrange(grid, g=G), ALU.is_equal)); last()
            done(ts(neg[:, :, 1:G1], same[:, :, 1:G1], -NEG, NEG, ALU.mult, ALU.add))
            cp(run_first[:, :], dst_i[:, 0:1])
            cp(run_f[:, 0:1], dst_i[:, 0:1])
            cp(run_f[:, 1:2], dst_before_i[:, 0:1])
            cp(run_f[:, 2:3], dst_i[:, J - 1:J])
            done(cp(run_f[:, 3:4], run_next[:, 0:1])); last()
            cp(cont_in[:, 0, :], run_f[:, 1:2].to_broadcast([P, P]))
            cp(cont_in[:, 1, :], run_f[:, 2:3].to_broadcast([P, P])).then_inc(s_contT, 1)
            done(tt(split_hit[:, 0:SROWS], dst_i[:, 0:SROWS], run_f[:, 0:1].to_broadcast([P, SROWS]), ALU.is_equal)); last()
            done(red(run_f[:, 4:5], split_hit[:, 0:SROWS], AX.X, ALU.add)); last()
            rest = J - SROWS
            done(tt(split_hit[:, 0:rest], dst_i[:, SROWS:J], run_f[:, 0:1].to_broadcast([P, rest]), ALU.is_equal)); last()
            done(red(run_f[:, 5:6], split_hit[:, 0:rest], AX.X, ALU.add)); last()
            dve.wait_ge(s_const, 80)
            done(tt(run_f[:, 4:5], run_f[:, 4:5], run_f[:, 5:6], ALU.add)); last()
            done(tt(run_f[:, 4:5], run_f[:, 4:5], run_no[:, 0:1], ALU.add)); last()
            done(ts(run_f[:, 4:5], run_f[:, 4:5], -1.0, None, ALU.add)); last()
            cp(run_row[:, :], run_f[:, 4:5])
            done(tt(run_f[:, 5:6], run_f[:, 0:1], run_f[:, 1:2], ALU.is_equal))
            done(tt(run_f[:, 6:7], run_f[:, 0:1], run_f[:, 3:4], ALU.not_equal)); last()
            done(tt(run_f[:, 5:6], run_f[:, 5:6], run_f[:, 6:7], ALU.mult)); last()
            done(tt(run_f[:, 6:7], run_f[:, 4:5], run_no[:, 1:2], ALU.subtract)); last()
            done(tt(run_f[:, 6:7], run_f[:, 6:7], run_f[:, 5:6], ALU.mult)); last()
            done(tt(mend_row[:, :], run_f[:, 6:7], run_no[:, 1:2], ALU.add)); last()
            dve.wait_ge(s_contT, 2)
            done(cp(cont[:, :], pT[:, 0, 0:P])); last()
            done(tt(cont[:, :], cont[:, :], pT[:, 0, P:2 * P], ALU.is_equal)); last()
            ts(cont_neg[:, :], cont[:, :], -NEG, NEG, ALU.mult, ALU.add).then_inc(s_contT, 1)

            dve.wait_ge(s_src, 32)
            for n_i, tmp, out in ((pe_src, pe_tmp, pe_code), (pe_src_r, src_r_flat, src_r_flat)):
                done(ts(tmp, n_i, 1.0 / GB, -3.0 / GB, ALU.mult, ALU.add)); last()
                done(ts(tmp, tmp, ROUND, None, ALU.add)); last()
                if out is pe_code:
                    ts(out, tmp, -ROUND, None, ALU.add).then_inc(s_code_cut, 1)
                else:
                    done(ts(tmp, tmp, -ROUND, -float(GB), ALU.add, ALU.mult)); last()
                    done(tt(out, tmp, n_i, ALU.add)); last()

            dve.wait_ge(s_split_in, 16)
            for g in range(GROUPS):
                for b in range(g * GB, (g + 1) * GB):
                    done(tt(split_hit, split_all, node_no[:, b:b + 1].to_broadcast([P, SROWS]), ALU.is_le)); last()
                    done(red(ranks_f[:, 0, b:b + 1], split_hit, AX.X, ALU.add)); last()
                part = ranks_f[:, 0, g * GB:(g + 1) * GB]
                done(ts(part, part, float(SROWS - 1), None, ALU.min)); last()
                cp(search_row[:, g * GB:(g + 1) * GB], part).then_inc(s_srow, 1)
            dve.wait_ge(s_x, 16)
            layernorm(h[:], x[:], 0, done, last)
            ts(h[:], h[:], 0.0, None, ALU.max).then_inc(s_h, GROUPS)
            for g in range(GROUPS):
                sl = slice(g * GB, (g + 1) * GB)
                dve.wait_ge(s_searched[g], 16 * GB)
                done(tt(searched[:, sl, :], searched_i[:, sl, :], over(node_no[:, sl], SR), ALU.is_le)); last()
                done(red(ranks_f[:, 1, sl], searched[:, sl, :], AX.X, ALU.add)); last()
            done(ts(ranks_f[:, 0, :], ranks_f[:, 0, :], float(SR), None, ALU.mult)); last()
            done(tt(ranks_f[:, 0, :], ranks_f[:, 0, :], ranks_f[:, 1, :], ALU.add)); last()
            cp(ranks_i[:, 1, :], ranks_f[:, 3, :])
            cp(ranks_i[:, 0, :], ranks_f[:, 0, :]).then_inc(s_rank, 1)
            dve.wait_ge(s_rank_in, 16)
            done(cp(ranks_f[:, 1, :], ranks_i[:, 1, :])); last()
            done(tt(ranks_f[:, 2, :], ranks_f[:, 0, :], ranks_f[:, 1, :], ALU.is_equal)); last()
            done(ts(ranks_f[:, 3, :], ranks_f[:, 0, :], -1.0, float(ZERO_ROW + 1), ALU.mult, ALU.add)); last()
            done(tt(ranks_f[:, 3, :], ranks_f[:, 3, :], ranks_f[:, 2, :], ALU.mult)); last()
            done(tt(ranks_f[:, 0, :], ranks_f[:, 0, :], ranks_f[:, 3, :], ALU.add)); last()
            done(ts(last_edge[:, :], ranks_f[:, 0, :], -1.0, None, ALU.add)); last()
            done(ts(ranks_f[:, 3, :], node_no[:, :], float(EP), None, ALU.add)); last()
            done(tt(ranks_f[:, 3, :], ranks_f[:, 3, :], ranks_f[:, 1, :], ALU.subtract)); last()
            done(tt(ranks_f[:, 3, :], ranks_f[:, 3, :], ranks_f[:, 2, :], ALU.mult)); last()
            tt(first_edge[:, :], ranks_f[:, 1, :], ranks_f[:, 3, :], ALU.add).then_inc(s_index, 1)
            dve.wait_ge(s_index, 1)
            dve.sem_inc(s_masks, 1)
            prologue_steps = steps[0]

            flat3 = "p a b -> p (a b)"

            def build_one_hot(use, k):
                dve.wait_ge(s_code[k], (use + 1) * 16)
                dve.wait_ge(s_pg[k], use)
                for m in range(GB):
                    ins = ts(one_hot[k][:, m, :], code[k], code_no[:, m:m + 1], None, ALU.is_equal)
                ins.then_inc(s_hot[k], 1)

            def pick_rows(use, turn, turn_all, k):
                tt(pick[:], src_r[:, bass.ds(turn, 1), :].to_broadcast([P, GB, GE]), over(pick_no[:, :], GE),
                   ALU.is_equal).then_inc(s_pick, 1)
                dve.wait_ge(s_pick, turn_all * GB + 1)
                dve.wait_ge(s_pg[k], use + 1)
                dve.sem_inc(s_passed, 1)
                rows = xl[:, k, GD:G, :]
                for r in range(GB):
                    ins = dve.copy_predicated(rows, over(pick[:, r, :], C), pG[:, k * GE:(k + 1) * GE, r * C:(r + 1) * C])
                    ins.then_inc(s_pick if r < GB - 1 else s_picked[k], 1)
                    if r < GB - 1:
                        dve.wait_ge(s_pick, turn_all * GB + (r + 2))
                        dve.sem_inc(s_passed, 1)
                dve.wait_ge(s_picked[k], use + 1)

            def cut_parts(g, base):
                done, last, steps = chain(dve, s_part_steps, base + g * 4)
                src = XL[:, g * GB:(g + 1) * GB, :].rearrange("p b c -> p (b c)")
                sl = slice(g * GB * C, (g + 1) * GB * C)
                done(cp(xl_part[0][:, sl], src)); last()
                done(tt(left[:, 0, :], src, xl_part[0][:, sl], ALU.subtract)); last()
                done(cp(xl_part[1][:, sl], left[:, 0, :])); last()
                done(tt(left[:, 1, :], left[:, 0, :], xl_part[1][:, sl], ALU.subtract)); last()
                cp(xl_part[2][:, sl], left[:, 1, :]).then_inc(s_parts, 1)

            def attention_turn(l, i, k):
                use = l * PAIRS + i
                turn_all = l * TURNS + 2 * i + k
                done, last, steps = chain(dve, s_turn, turn_all * K_TURN)
                dve.wait_ge(s_turned[k], use + 1)
                done(cp(xr_in[:, :, 0:1], xr_out[:, :, G:G1])); last()
                dve.wait_ge(s_same, turn_all + 1)
                dve.tensor_tensor_scan(xr_out[:].rearrange(flat3), same_c[:].rearrange(flat3), xr_in[:].rearrange(flat3),
                                       0.0, ALU.mult, ALU.add).then_inc(s_xr, 1)
                dve.wait_ge(s_xr, turn_all + 1)
                dve.wait_ge(s_xl[k], (use + 1) * (16 * GD))
                pick_rows(use, 2 * i + k, turn_all, k)
                done(tt(s[:], xl[:, k], xr_out[:, :, 1:G1].rearrange("p c g -> p g c"), ALU.add)); last()
                done(dve.scalar_tensor_tensor(out=lr[:], in0=s[:], scalar=SLOPE, in1=s[:], op0=ALU.mult, op1=ALU.max)); last()
                done(tt(s[:], lr[:], blocks(a_all[:, bass.ds(l * C, C)], G), ALU.mult))
                done(cp(e_in[:, :, 0:1], m_run[:, :, G:G1])); last()
                done(red(e_in[:, :, 1:G1].rearrange("p h g -> p g h"), s[:].rearrange("p g (h o) -> p g h o", h=H), AX.X, ALU.add)); last()
                dve.wait_ge(s_neg, turn_all + 1)
                dve.wait_ge(s_out, turn_all)
                done(dve.tensor_tensor_scan(m_run[:].rearrange(flat3), neg_h[:].rearrange(flat3), e_in[:].rearrange(flat3),
                                            0.0, ALU.add, ALU.max)); last()
                tt(w_arg[:], e_in[:, :, 1:G1], m_run[:, :, 1:G1], ALU.subtract).then_inc(s_warg, 1)
                done(tt(f_arg[:], m_run[:, :, 0:G], m_run[:, :, 1:G1], ALU.subtract)); last()
                tt(f_arg[:], f_arg[:], neg_h[:, :, 1:G1], ALU.add).then_inc(s_farg, 1)
                done(cp(v_in[:, :, 0:1], s_run[:, :, G:G1])); last()
                build_one_hot(use + 1, k)
                dve.wait_ge(s_w, turn_all + 1)
                tt(v_heads[:, :, 0:O, 1:G1].rearrange("p h o g -> p g h o"),
                   xl[:, k].rearrange("p g (h o) -> p g h o", h=H),
                   over(v_heads[:, :, O, 1:G1].rearrange("p h g -> p g h"), O), ALU.mult).then_inc(s_used[k], 1)
                dve.wait_ge(s_used[k], use + 1)
                dve.wait_ge(s_f, turn_all + 1)
                dve.tensor_tensor_scan(s_run[:].rearrange(flat3), f_all[:].rearrange(flat3), v_in[:].rearrange(flat3),
                                       0.0, ALU.mult, ALU.add).then_inc(s_sums, 1)
                dve.wait_ge(s_sums, turn_all + 1)
                return steps[0]

            for k in range(2):
                build_one_hot(0, k)
            with dve.Fori(0, LAYERS) as l:
                for g in range(GROUPS):
                    dve.wait_ge(s_xlxr, l * GROUPS + (g + 1))
                    cut_parts(g, l * (4 * GROUPS))
                dve.wait_ge(s_xr_first, (l + 1) * 16)
                dve.memset(m_run[:], NEG)
                dve.memset(s_run[:], 0.0)
                cp(xr_out[:, :, G:G1], xr_first[:, :].unsqueeze(2)).then_inc(s_start, 1)
                dve.wait_ge(s_start, l + 1)
                dve.sem_inc(s_passed, 1)
                with dve.Fori(0, PAIRS) as i:
                    for k in range(2):
                        n = attention_turn(l, i, k)
                        assert n == K_TURN, n
                done, last, steps = chain(dve, s_ends, l * K_ENDS)
                done(cp(fin_s[:, :], s_run[:, :, G]))
                cp(fin_m[:], over(m_run[:, :, G], HO)).then_inc(s_fin, 1)
                last()
                dve.wait_ge(s_finT, l + 1)
                done(dve.tensor_tensor_scan(rm[0:V, 1:P + 1], cont_neg[0:V, :], pT[0:V, 0, P:2 * P], NEG, ALU.add, ALU.max)); last()
                done(tt(ra[0:V, 0, :], rm[0:V, 0:P], rm[0:V, 1:P + 1], ALU.subtract)); last()
                done(tt(ra[0:V, 0, :], ra[0:V, 0, :], cont_neg[0:V, :], ALU.add)); last()
                tt(ra[0:V, 1, :], pT[0:V, 0, P:2 * P], rm[0:V, 1:P + 1], ALU.subtract).then_inc(s_rarg, 1)
                dve.wait_ge(s_rexp, l + 1)
                done(tt(rt[0:V, :], rt[0:V, :], pT[0:V, 0, 0:P], ALU.mult)); last()
                dve.tensor_tensor_scan(rs[0:V, 1:P + 1], rf[0:V, :], rt[0:V, :], 0.0, ALU.mult, ALU.add).then_inc(s_rsc, 1)
                dve.wait_ge(s_rback, l + 1)
                done(cp(carry_in[:], pP[:, 0, 0:2 * P].rearrange("p (a v) -> p a v", a=2)[:, :, 0:V])); last()
                dve.wait_ge(s_local, (l + 1) * 16)
                carried_m = carry_in[:, 1, :].rearrange("p (h o) -> p h o", h=H)
                done(tt(mm[:], carried_m, over(local[:, V:ROW], HO), ALU.max)); last()
                mw_h = mw[:].rearrange("p a (h o) -> p a h o", h=H)
                tt(mw_h[:, 0], over(local[:, V:ROW], HO), mm[:], ALU.subtract)
                tt(mw_h[:, 1], carried_m, mm[:], ALU.subtract).then_inc(s_marg, 1)
                dve.wait_ge(s_mexp, l + 1)
                done(tt(mw[:, 0, :], mw[:, 0, :], local[:, 0:V], ALU.mult))
                done(tt(mw[:, 1, :], mw[:, 1, :], carry_in[:, 0, :], ALU.mult)); last()
                done(cp(mend[:, V:ROW], mm[:, :, 0]))
                done(tt(mend[:, 0:V], mw[:, 0, :], mw[:, 1, :], ALU.add)); last()
                dve.sem_inc(s_mend, 1)
                assert steps[0] == K_ENDS, steps[0]
                done, last, steps = chain(dve, s_node, l * K_NODE)
                for g in range(GROUPS):
                    sl = slice(g * GB, (g + 1) * GB)
                    heads = node_rows[:, sl, 0:V].rearrange("p b (h o) -> p b h o", h=H)
                    dve.wait_ge(s_nrow[g], (l + 1) * (16 * GB))
                    done(ts(recip[:, sl, :], heads[:, :, :, O], 1e-16, None, ALU.add)); last()
                    done(dve.reciprocal(recip[:, sl, :], recip[:, sl, :])); last()
                    for b in range(g * GB, (g + 1) * GB):
                        one = node_rows[:, b, 0:V].rearrange("p (h o) -> p h o", h=H)[:, :, 0:O]
                        ins = tt(h[:, b, :].rearrange("p (h o) -> p h o", h=H), one, over(recip[:, b, :], O), ALU.mult)
                    done(ins); last()
                    done(tt(h[:, sl, :], h[:, sl, :], blocks(b_all[:, bass.ds(l * C, C)], GB), ALU.add)); last()
                    ts(h[:, sl, :], h[:, sl, :], floor_all[:, bass.ds(l, 1)], None, ALU.max).then_inc(s_h, 1)
                assert steps[0] == K_NODE, steps[0]

            dve.wait_ge(s_h, (LAYERS + 1) * GROUPS)
            done, last, steps = chain(dve, s_pro, prologue_steps)
            done(tt(x[:], x[:], h[:], ALU.add)); last()
            layernorm(h[:], x[:], 2, done, last)
            ts(h[:], h[:], 0.0, None, ALU.max).then_inc(s_gin, 1)
            dve.wait_ge(s_gin, 1)
            tt(XL[:], h[:], blocks(be_all[:, :], B), ALU.add).then_inc(s_gin, 1)
            tt(x[:], x[:], blocks(b2_all[:, :], B), ALU.add).then_inc(s_gin, 1)
            dve.wait_ge(s_gin, K_LIN)
            for g in range(GROUPS):
                cut_parts(g, LAYERS * 4 * GROUPS)
            dve.memset(s_run[:], 0.0).then_inc(s_gin, 1)
            dve.wait_ge(s_gin, K_LIN + 1)

            def linear_turn(i, k):
                use = i + LAYERS * PAIRS
                turn = 2 * i + k
                turn_all = 2 * i + (k + LAYERS * TURNS)
                dve.wait_ge(s_xl[k], (use + 1) * (16 * GD))
                pick_rows(use, turn, turn_all, k)
                dve.wait_ge(s_ea[k], i + 1)
                dve.wait_ge(s_lin_relu, turn)
                tt(s[:].rearrange("p g c -> p (g c)"), xl[:, k].rearrange("p g c -> p (g c)"), pE[:, :], ALU.add).then_inc(s_lin, 1)
                dve.wait_ge(s_lin, turn + 1)
                dve.sem_inc(s_used[k], 1)
                dve.sem_inc(s_ea_used, 1)
                build_one_hot(use + 1, k)
                cp(v_lin[:, :, 0:1], lin_run[:, :, G:G1]).then_inc(s_turn, 1)
                dve.wait_ge(s_turn, LAYERS * TURNS * K_TURN + 2 * i + (k + 1))
                dve.wait_ge(s_lin_relu, turn + 1)
                dve.wait_ge(s_same, turn_all + 1)
                dve.wait_ge(s_out, turn_all)
                dve.tensor_tensor_scan(lin_run.rearrange(flat3), same_c[:].rearrange(flat3), v_lin.rearrange(flat3),
                                       0.0, ALU.mult, ALU.add).then_inc(s_sums, 1)
                dve.wait_ge(s_sums, turn_all + 1)

            with dve.Fori(0, PAIRS) as i:
                for k in range(2):
                    linear_turn(i, k)
            cp(fin_s[:, 0:C], lin_run[:, :, G]).then_inc(s_fin, 1)
            dve.wait_ge(s_finT, LAYERS + 1)
            dve.tensor_tensor_scan(rs[0:C, 1:P + 1], cont[0:C, :], pT[0:C, 0, 0:P], 0.0, ALU.mult, ALU.add).then_inc(s_rsc, 1)
            dve.wait_ge(s_rback, LAYERS + 1)
            dve.wait_ge(s_local, (LAYERS + 1) * 16)
            tt(mend[:, 0:C], local[:, 0:C], pP[:, 0, 0:C], ALU.add).then_inc(s_mend, 1)
            for g in range(GROUPS):
                sl = slice(g * GB, (g + 1) * GB)
                dve.wait_ge(s_nrow[g], (LAYERS + 1) * (16 * GB))
                tt(h[:, sl, :], h[:, sl, :], node_rows[:, sl, 0:C], ALU.add).then_inc(s_z, 1)
            u3 = uT.rearrange("c (b q) -> c b q", b=B)
            z3 = zT.rearrange("c (b q) -> c b q", b=B)

            def node_sum(col, v3):
                done(red(bn[:, col:col + 1], v3[:, :, 0:P - 1], AX.XY, ALU.add))
                done(red(bn[:, col + 1:col + 2], v3[:, 0:LAST_PAD, P - 1], AX.X, ALU.add)); last()
                done(tt(bn[:, col:col + 1], bn[:, col:col + 1], bn[:, col + 1:col + 2], ALU.add)); last()

            dve.wait_ge(s_uc, (B + 3) // 4)
            dve.wait_ge(s_weights, 16 * 8)
            node_sum(0, u3)
            done(ts(bn[:, 2:3], bn[:, 0:1], 1.0 / N, None, ALU.mult)); last()
            ts(uT, uT, bn[:, 2:3], None, ALU.subtract).then_inc(s_sq, 1)
            dve.wait_ge(s_sq, 2)
            node_sum(0, z3)
            ts(bn[:, 4:5], bn[:, 0:1], 1.0 / N, EPS, ALU.mult, ALU.add).then_inc(s_bnstd, 1)
            dve.wait_ge(s_bnstd, 2)
            done(dve.reciprocal(bn[:, 6:7], bn[:, 5:6])); last()
            tt(bn[:, 7:8], bn[:, 6:7], cols[:, 1:2], ALU.mult).then_inc(s_bnp, 1)
            for g in range(GROUPS):
                dve.wait_ge(s_o, g + 1)
                for half, (lo, n) in enumerate(((0, 4), (4, 3))):
                    sl = slice(g * GB + lo, g * GB + lo + n)
                    ins = tt(XR[:, sl, :], pT[:, half, 0:n * P].rearrange("p (i q) -> p i q", i=n)[:, :, 0:C], x[:, sl, :], ALU.add)
                ins.then_inc(s_final, 1)


def kernel(**inputs):
    import concourse.bacc as bacc
    from concourse.bass_utils import run_bass_kernel_spmd

    nc = bacc.Bacc("TRN2", target_bir_lowering=False, num_devices=1)
    arr = {k: np.asarray(v) for k, v in inputs.items()}
    x_nodes = np.zeros((NB, C), np.float32)
    x_nodes[:N] = arr["x"]
    src = np.zeros(EP, np.int32)
    src[:E] = arr["src"]
    dst = np.full(EP + 2, N, np.int32)
    dst[0] = -1
    dst[1:1 + E] = arr["dst"]
    dst[-1] = N + 1
    attr = np.zeros((EP, KE), np.float32)
    attr[:E] = arr["edge_attr_16"]
    attr_t = attr.reshape(P, TURNS, 2, 8, KE).transpose(1, 3, 4, 2, 0).reshape(TURNS, P, 2 * P)
    w = [np.concatenate([arr[f"L0_gnn_Wl{k}"], arr[f"L0_gnn_Wr{k}"]], axis=1) for k in (1, 2, 3)]
    data = {
        "x_nodes": x_nodes,
        "src_edges": src.reshape(P, J),
        "dst_edges": dst[1:1 + EP].reshape(P, J),
        "dst_before": dst[0:EP].reshape(P, J),
        "dst_next_run": dst[1 + J::J].reshape(P, 1),
        "dst_rows": dst[1:1 + EP].reshape(SROWS, SR),
        "attr_t": attr_t,
        "w_gat": np.concatenate(w, axis=1),
        "a_rows": np.concatenate([arr[f"L0_gnn_a{k}"].reshape(C) for k in (1, 2, 3)]),
        "b_rows": np.concatenate([arr[f"L0_gnn_b{k}"] for k in (1, 2, 3)]),
        "w_edge_t": arr["L1_gnn_W_edge"].T,
        "w1_t": arr["L1_gnn_W1"].T,
        "w2_t": arr["L1_gnn_W2"].T,
        "channel_cols": np.stack([arr["L1_gnn_b1"], arr["L1_gnn_gamma"], arr["L1_gnn_beta"]], axis=1),
        "b_edge": arr["L1_gnn_b_edge"],
        "b2": arr["L1_gnn_b2"],
        "src_pe_places": np.stack([src.reshape(P, TURNS, G)[:, :, GD + a] for a in range(GE)]).transpose(2, 0, 1).reshape(TURNS, EC),
        "src_pe_edges": src.reshape(P, TURNS, G)[:, :, GD:].reshape(P, TURNS * GE),
        "code_no": np.arange(P * GB, dtype=np.float32).reshape(P, GB),
        "pick_no": np.tile(np.arange(GB, dtype=np.float32), (P, 1)),
        "identity": np.eye(P, dtype=np.float32),
        "node_no": np.arange(NB, dtype=np.float32).reshape(P, B),
        "run_no": np.stack([np.arange(P, dtype=np.float32) * J, np.arange(P, dtype=np.float32) + (EP + 1)], axis=1),
    }
    data = {k: np.ascontiguousarray(v) for k, v in data.items()}
    t = {k: nc.dram_tensor(k, v.shape, mybir.dt.from_np(v.dtype), kind="ExternalInput").ap() for k, v in data.items()}
    t["out"] = nc.dram_tensor("out", (NB, C), F32, kind="ExternalOutput").ap()
    build(nc, t)
    result = run_bass_kernel_spmd(nc, [data], core_ids=[0])
    return result.results[0]["out"][:N]
```
